# Optimizing a Trainium2 kernel written in Bass

```python
import numpy as np
import jax
import jax.numpy as jnp

def _softmax(x, axis=-1):
    return jax.nn.softmax(x, axis=axis)

def _gelu(x):
    return jax.nn.gelu(x, approximate=True)

def _silu(x):
    return jax.nn.silu(x)

def _sigmoid(x):
    return jax.nn.sigmoid(x)

def _layernorm(x, axis=-1, eps=1e-05):
    m = jnp.mean(x, axis=axis, keepdims=True)
    v = jnp.var(x, axis=axis, keepdims=True)
    return (x - m) / jnp.sqrt(v + eps)

def _scatter_add(tgt, idx, src, axis=0):
    return tgt.at[idx].add(src)

def _segment_sum(src, seg, n):
    return jax.ops.segment_sum(src, seg, n)
kernel_name = 'mk_seq_postln_d1_jaxref_r8_8e74b9'

def setup_inputs(seed: int=0):
    np.random.seed(seed)
    _w = jnp.asarray

    def _L0_attn_setup():
        import jax, jax.numpy as jnp
        import numpy as np
        H_M, P_M, G_M, N_M, K_CONV, CHUNK = (128, 64, 8, 128, 4, 128)
        D_MODEL = 512
        D_INNER = H_M * P_M
        CONV_DIM = D_INNER + 2 * G_M * N_M
        PROJ_DIM = D_INNER + CONV_DIM + H_M
        EPS = 1e-05

        def segsum(x):
            l = x.shape[-1]
            xe = jnp.broadcast_to(x[..., None], x.shape + (l,))
            m1 = jnp.tril(jnp.ones((l, l), dtype=bool), -1)
            s = jnp.cumsum(jnp.where(m1, xe, 0.0), axis=-2)
            m2 = jnp.tril(jnp.ones((l, l), dtype=bool), 0)
            return jnp.where(m2, s, -jnp.inf)

        def causal_conv(x, w, bconv):
            k = w.shape[1]
            s = x.shape[1]
            xp = jnp.pad(x, ((0, 0), (k - 1, 0), (0, 0)))
            y = sum((xp[:, i:i + s, :] * w[:, i] for i in range(k)))
            return y + bconv
        key = jax.random.key(seed)
        ks = jax.random.split(key, 8)
        B_, S = (1, 256)
        sc = 0.02
        return {'x': jax.random.normal(ks[0], (B_, S, D_MODEL), dtype=jnp.float32), 'norm_w': jnp.ones((D_MODEL,), dtype=jnp.float32), 'in_proj_w': jax.random.normal(ks[1], (PROJ_DIM, D_MODEL), dtype=jnp.float32) * sc, 'conv_w': jax.random.normal(ks[2], (CONV_DIM, K_CONV), dtype=jnp.float32) * 0.2, 'conv_b': jnp.zeros((CONV_DIM,), dtype=jnp.float32), 'dt_bias': jax.random.uniform(ks[3], (H_M,), dtype=jnp.float32) * 0.1, 'A_log': jnp.log(1.0 + 15.0 * jax.random.uniform(ks[4], (H_M,), dtype=jnp.float32)), 'Dp': jnp.ones((H_M,), dtype=jnp.float32), 'gnorm_w': jnp.ones((D_INNER,), dtype=jnp.float32), 'out_proj_w': jax.random.normal(ks[5], (D_MODEL, D_INNER), dtype=jnp.float32) * sc}
    _L0_attn_in = _L0_attn_setup()

    def _L0_ffn_setup():
        import jax, jax.numpy as jnp
        import numpy as np
        GROUP_SIZE = 128

        def dequantize(imatrix, scales, zeros, group_size, out_dtype):
            rs = jnp.repeat(scales, group_size, axis=0)
            rz = jnp.repeat(zeros, group_size, axis=0)
            return ((imatrix.astype(rs.dtype) - rz.astype(rs.dtype)) * rs).astype(out_dtype)
        key = jax.random.key(seed)
        ks = jax.random.split(key, 10)
        H, I, G = (512, 1792, GROUP_SIZE)
        B, S = (4, 256)
        x = jax.random.normal(ks[0], (B, S, H), dtype=jnp.float32)
        gate_w = jax.random.randint(ks[1], (H, I), 0, 16, dtype=jnp.int32)
        gate_z = jax.random.randint(ks[2], (H // G, I), 0, 16, dtype=jnp.int32)
        gate_s = jax.random.uniform(ks[3], (H // G, I), dtype=jnp.float32) * 0.01
        up_w = jax.random.randint(ks[4], (H, I), 0, 16, dtype=jnp.int32)
        up_z = jax.random.randint(ks[5], (H // G, I), 0, 16, dtype=jnp.int32)
        up_s = jax.random.uniform(ks[6], (H // G, I), dtype=jnp.float32) * 0.01
        down_w = jax.random.randint(ks[7], (I, H), 0, 16, dtype=jnp.int32)
        down_z = jax.random.randint(ks[8], (I // G, H), 0, 16, dtype=jnp.int32)
        down_s = jax.random.uniform(ks[9], (I // G, H), dtype=jnp.float32) * 0.01
        return {'x': x, 'gate_w': gate_w, 'gate_z': gate_z, 'gate_s': gate_s, 'up_w': up_w, 'up_z': up_z, 'up_s': up_s, 'down_w': down_w, 'down_z': down_z, 'down_s': down_s}
    _L0_ffn_in = _L0_ffn_setup()
    _d = {'L0_attn_x': _L0_attn_in['x'], 'L0_attn_norm_w': _L0_attn_in['norm_w'], 'L0_attn_in_proj_w': _L0_attn_in['in_proj_w'], 'L0_attn_conv_w': _L0_attn_in['conv_w'], 'L0_attn_conv_b': _L0_attn_in['conv_b'], 'L0_attn_dt_bias': _L0_attn_in['dt_bias'], 'L0_attn_A_log': _L0_attn_in['A_log'], 'L0_attn_Dp': _L0_attn_in['Dp'], 'L0_attn_gnorm_w': _L0_attn_in['gnorm_w'], 'L0_attn_out_proj_w': _L0_attn_in['out_proj_w'], 'L0_ffn_gate_w': _L0_ffn_in['gate_w'], 'L0_ffn_gate_z': _L0_ffn_in['gate_z'], 'L0_ffn_gate_s': _L0_ffn_in['gate_s'], 'L0_ffn_up_w': _L0_ffn_in['up_w'], 'L0_ffn_up_z': _L0_ffn_in['up_z'], 'L0_ffn_up_s': _L0_ffn_in['up_s'], 'L0_ffn_down_w': _L0_ffn_in['down_w'], 'L0_ffn_down_z': _L0_ffn_in['down_z'], 'L0_ffn_down_s': _L0_ffn_in['down_s']}
    _x0 = _d['L0_attn_x']
    _d['L0_attn_x'] = jax.random.normal(jax.random.fold_in(jax.random.key(seed), 1), (2, 512, 512), dtype=_x0.dtype)
    del _x0
    return _d

def reference(L0_attn_x, L0_attn_norm_w, L0_attn_in_proj_w, L0_attn_conv_w, L0_attn_conv_b, L0_attn_dt_bias, L0_attn_A_log, L0_attn_Dp, L0_attn_gnorm_w, L0_attn_out_proj_w, L0_ffn_gate_w, L0_ffn_gate_z, L0_ffn_gate_s, L0_ffn_up_w, L0_ffn_up_z, L0_ffn_up_s, L0_ffn_down_w, L0_ffn_down_z, L0_ffn_down_s):

    def _L0_attn_ref(x, norm_w, in_proj_w, conv_w, conv_b, dt_bias, A_log, Dp, gnorm_w, out_proj_w):
        import jax, jax.numpy as jnp
        import numpy as np
        H_M, P_M, G_M, N_M, K_CONV, CHUNK = (128, 64, 8, 128, 4, 128)
        D_MODEL = 512
        D_INNER = H_M * P_M
        CONV_DIM = D_INNER + 2 * G_M * N_M
        PROJ_DIM = D_INNER + CONV_DIM + H_M
        EPS = 1e-05

        def segsum(x):
            l = x.shape[-1]
            xe = jnp.broadcast_to(x[..., None], x.shape + (l,))
            m1 = jnp.tril(jnp.ones((l, l), dtype=bool), -1)
            s = jnp.cumsum(jnp.where(m1, xe, 0.0), axis=-2)
            m2 = jnp.tril(jnp.ones((l, l), dtype=bool), 0)
            return jnp.where(m2, s, -jnp.inf)

        def causal_conv(x, w, bconv):
            k = w.shape[1]
            s = x.shape[1]
            xp = jnp.pad(x, ((0, 0), (k - 1, 0), (0, 0)))
            y = sum((xp[:, i:i + s, :] * w[:, i] for i in range(k)))
            return y + bconv
        b, s, _ = x.shape
        residual = x
        h = x * jax.lax.rsqrt(jnp.mean(x * x, axis=-1, keepdims=True) + EPS) * norm_w
        proj = jnp.einsum('bsd,od->bso', h, in_proj_w)
        gate = proj[..., :D_INNER]
        hBC = proj[..., D_INNER:D_INNER + CONV_DIM]
        dt = proj[..., D_INNER + CONV_DIM:]
        hBC = jax.nn.silu(causal_conv(hBC, conv_w, conv_b))
        hid = hBC[..., :D_INNER].reshape(b, s, H_M, P_M)
        B = hBC[..., D_INNER:D_INNER + G_M * N_M].reshape(b, s, G_M, N_M)
        C = hBC[..., D_INNER + G_M * N_M:].reshape(b, s, G_M, N_M)
        dt = jax.nn.softplus(dt + dt_bias)
        A = -jnp.exp(A_log)
        pad = -s % CHUNK
        D_res = Dp[None, None, :, None] * hid
        hid_dt = hid * dt[..., None]
        A_full = A[None, None, :] * dt

        def padseq(t):
            return jnp.pad(t, [(0, 0), (0, pad)] + [(0, 0)] * (t.ndim - 2))
        hid_dt, A_full, Bp, Cp = (padseq(hid_dt), padseq(A_full), padseq(B), padseq(C))
        S = s + pad
        c, l = (S // CHUNK, CHUNK)
        hc = hid_dt.reshape(b, c, l, H_M, P_M)
        Ac = A_full.reshape(b, c, l, H_M).transpose(0, 3, 1, 2)
        rep = H_M // G_M
        Bh = jnp.repeat(Bp.reshape(b, c, l, G_M, N_M), rep, axis=3)
        Ch = jnp.repeat(Cp.reshape(b, c, l, G_M, N_M), rep, axis=3)
        A_cs = jnp.cumsum(Ac, axis=-1)
        L = jnp.exp(segsum(Ac))
        M = jnp.einsum('bcihn,bcjhn->bcijh', Ch, Bh) * jnp.transpose(L, (0, 2, 3, 4, 1))
        Y_diag = jnp.einsum('bcijh,bcjhp->bcihp', M, hc)
        decay_states = jnp.exp(A_cs[..., -1:] - A_cs)
        states = jnp.einsum('bclhn,bhcl,bclhp->bchpn', Bh, decay_states, hc)
        A_last = jnp.pad(A_cs[..., -1], ((0, 0), (0, 0), (1, 0)))
        decay_chunk = jnp.exp(segsum(A_last))
        states_cat = jnp.concatenate([jnp.zeros_like(states[:, :1]), states], axis=1)
        prev_states = jnp.einsum('bhij,bjhpn->bihpn', decay_chunk, states_cat)[:, :-1]
        Y_off = jnp.einsum('bclhn,bchpn,bhcl->bclhp', Ch, prev_states, jnp.exp(A_cs))
        y = (Y_diag + Y_off).reshape(b, S, H_M, P_M)[:, :s] + D_res
        y = y.reshape(b, s, D_INNER)
        yg = y * jax.nn.silu(gate)
        gsz = D_INNER // G_M
        ygr = yg.reshape(b, s, G_M, gsz)
        ygr = ygr * jax.lax.rsqrt(jnp.mean(ygr * ygr, axis=-1, keepdims=True) + EPS)
        y = ygr.reshape(b, s, D_INNER) * gnorm_w
        out = jnp.einsum('bsd,od->bso', y, out_proj_w)
        return residual + out

    def _L0_ffn_ref(x, gate_w, gate_z, gate_s, up_w, up_z, up_s, down_w, down_z, down_s):
        import jax, jax.numpy as jnp
        import numpy as np
        GROUP_SIZE = 128

        def dequantize(imatrix, scales, zeros, group_size, out_dtype):
            rs = jnp.repeat(scales, group_size, axis=0)
            rz = jnp.repeat(zeros, group_size, axis=0)
            return ((imatrix.astype(rs.dtype) - rz.astype(rs.dtype)) * rs).astype(out_dtype)
        dt = x.dtype
        gate_proj = dequantize(gate_w, gate_s, gate_z, GROUP_SIZE, dt)
        up_proj = dequantize(up_w, up_s, up_z, GROUP_SIZE, dt)
        down_proj = dequantize(down_w, down_s, down_z, GROUP_SIZE, dt)
        gate = jax.nn.silu(jnp.dot(x, gate_proj))
        up = jnp.dot(x, up_proj)
        return jnp.dot(gate * up, down_proj)
    x = L0_attn_x
    x = _layernorm(x + _L0_attn_ref(x, L0_attn_norm_w, L0_attn_in_proj_w, L0_attn_conv_w, L0_attn_conv_b, L0_attn_dt_bias, L0_attn_A_log, L0_attn_Dp, L0_attn_gnorm_w, L0_attn_out_proj_w), axis=-1)
    x = _layernorm(x + _L0_ffn_ref(x, L0_ffn_gate_w, L0_ffn_gate_z, L0_ffn_gate_s, L0_ffn_up_w, L0_ffn_up_z, L0_ffn_up_s, L0_ffn_down_w, L0_ffn_down_z, L0_ffn_down_s), axis=-1)
    return x

_drawn_inputs = setup_inputs


def setup_inputs(seed=0):
    import zlib

    import numpy as np

    out = dict(_drawn_inputs(seed))
    spreads = {'L0_attn_norm_w': (1.0, 0.2),
     'L0_attn_conv_b': (0.0, 0.1),
     'L0_attn_Dp': (1.0, 0.2),
     'L0_attn_gnorm_w': (1.0, 0.2)}
    factors = {}
    for name, (base, spread) in spreads.items():
        noise = np.random.default_rng([zlib.crc32(name.encode()), seed]).standard_normal(out[name].shape)
        drawn = base * np.exp(spread * noise) if base else spread * noise
        out[name] = jnp.asarray(drawn.astype(out[name].dtype))
    for name, factor in factors.items():
        out[name] = (out[name] * factor).astype(out[name].dtype)
    return out
```

```python
from contextlib import ExitStack

import concourse.bass as bass
from concourse import mybir

F32 = mybir.dt.float32
BF16 = mybir.dt.bfloat16
I32 = mybir.dt.int32
ALU = mybir.AluOpType
ACT = mybir.ActivationFunctionType

P = 128
D = 512
KD = D // P
H, HP, G = 128, 64, 8
HG = H // G
T = 1024
TB = 512
CH = TB // P
NT = T // P
NPAIR = HG // 2
STEPS = 2 * G
GC = NPAIR * P
EPS = 1e-5
TINY = 1e-30
ABOVE = -1e9
BIG = 3e38

PROJ = [
    [("h", 0), ("h", 1), ("B", 0), ("g", 0), ("g", 1)],
    [("h", 2), ("h", 3), ("C", 0), ("g", 2), ("g", 3)],
    [("h", 4), ("h", 5), ("g", 4), ("g", 5)],
    [("h", 6), ("h", 7), ("g", 6), ("g", 7)],
]
ORDER = [x for row in PROJ for x in row]
NB = len(ORDER)
FIRST = [sum(len(r) for r in PROJ[:c]) for c in range(CH)]
CONV = [x for x in ORDER if x[0] != "g"]
GATE = [x for x in ORDER if x[0] == "g"]
NC, NG = len(CONV), len(GATE)
RING = 6
STAGE = 3

PROJ_DT = 2 * H * HP + 2 * G * P
FI = 1792
NF = FI // P


def count(value):
    return max(value, 0) if isinstance(value, int) else value


def build(nc, x, w_in, w_dt, convp, dpar, w_out, norm_w, dt_bias, a_log, wgu, zgu, sgu, wdn, zdn, sdn, out):
    acs_dram = nc.dram_tensor("acs_parts", [3, H, T], BF16, kind="Internal").ap()
    b_dram = nc.dram_tensor("b_parts", [3, H, T], BF16, kind="Internal").ap()
    dec_dram = nc.dram_tensor("chunk_decay", [H, NT], F32, kind="Internal").ap()
    with ExitStack() as ctx:
        banks = [ctx.enter_context(nc.psum_tensor(f"bank{i}", [P, 512], F32)) for i in range(8)]
        acc = ctx.enter_context(nc.sbuf_tensor("acc", [P, NT, D], F32))
        ident = ctx.enter_context(nc.sbuf_tensor("ident", [P, P], F32))
        stat = ctx.enter_context(nc.sbuf_tensor("stat", [P, NT, 6], F32))
        mvar = ctx.enter_context(nc.sbuf_tensor("mvar", [P, NT, 2], F32))
        with ExitStack() as inner:
            mixer(nc, inner, banks, acc, ident, stat, mvar, x, w_in, w_dt, convp, dpar, w_out, norm_w, dt_bias, a_log,
                  acs_dram, b_dram, dec_dram)
        with ExitStack() as inner:
            ffn(nc, inner, banks, acc, ident, stat, mvar, wgu, zgu, sgu, wdn, zdn, sdn, out)


def mixer(nc, ctx, banks, acc, ident, stat, mvar, x, w_in, w_dt, convp, dpar, w_out, norm_w, dt_bias, a_log,
          acs_dram, b_dram, dec_dram):
    def sb(name, shape, dt=F32):
        return ctx.enter_context(nc.sbuf_tensor(name, shape, dt))

    def sem(name):
        return ctx.enter_context(nc.semaphore(name))

    hT = sb("hT", [P, 2, KD, T], BF16)
    wst = sb("wst", [P, STAGE, KD * P])
    wr = sb("wr", [P, 2, RING, KD * P], BF16)
    wo = sb("wo", [P, 2, NPAIR, D], BF16)
    wost = sb("wost", [P, 4, D])
    hid = sb("hid", [P, 2, NPAIR, TB])
    gate = sb("gate", [P, 2, NPAIR, TB])
    bctmp = sb("bctmp", [P, 2, TB])
    bc = sb("bc", [P, 2, 2, 2, TB], BF16)
    cparam = sb("cparam", [P, 2, NC, 5])
    dparam = sb("dparam", [P, 2, 2 * NPAIR])
    sbt = sb("sbt", [P, 2, TB], BF16)
    t48 = sb("t48", [48, 2, TB], BF16)
    mv = sb("mv", [P, HG * P], BF16)
    psel = sb("psel", [48, NPAIR, P], BF16)
    dec = sb("dec", [P, 2, HG, CH])
    mf = sb("mf", [P, 2, 4 * P])
    mh = sb("mh", [P, 2, HG, P], BF16)
    hh = sb("hh", [P, 2, 4 * NPAIR, HP], BF16)
    x2f = sb("x2f", [P, 2, 512])
    x2 = sb("x2", [P, 2, GC], BF16)
    st = sb("st", [P, GC])
    sth = sb("sth", [P, 2, GC], BF16)
    ee = sb("ee", [P, GC])
    yt = sb("yt", [P, GC])
    yhl = sb("yhl", [P, 2, GC], BF16)
    ssb = sb("ssb", [P, 2, P], BF16)
    cbm = sb("cbm", [P, P])
    mask = sb("mask", [P, P])
    btok = sb("btok", [P, 2, P], BF16)
    w16 = sb("w16", [P, HG])
    identb = sb("identb", [P, P], BF16)
    onesb = sb("onesb", [P, 2], BF16)
    mhalf = sb("mhalf", [P, NT])
    ms = sb("ms", [P, NT])
    rs = sb("rs", [P, NT])
    small = sb("small", [P, KD + 4])

    bL = banks[0:2]
    bP = banks[2:4]
    bA, bB = banks[4], banks[5]
    bD = banks[6:8]

    names = """ld_x0 ld_x1 ld_small ld_wdt ld_step0 ld_step1 ld_cp0 ld_cp1 ld_dp0 ld_dp1 ld_mv st_scr
        pe_L pe_X pe_T pe_proj pe_E pe_Yo pe_ssq pe_out pe_St pe_Yd
        act_L act_Bt act_Th act_tap act_hs act_gate act_E act_X2h act_Mh act_Sh act_yh act_sq act_Wh act_Wo act_BCh
        dve_CB dve_M dve_Tl dve_X2 dve_conv dve_t1 dve_t2 dve_u dve_yg dve_yl dve_S dve_acc dve_ms dve_Wo dve_tap
        dve_w pool_Ml pool_X2l pool_Sd pool_Sl pool_Wl pool_BCl pool_sum pool_ssl pool_r
        pool_const pool_fill pool_ident pool_rs0 dve_hh dve_x2 dve_st act_sq0 dve_ms0 dve_xn
        pe_xt act_h dve_h pe_dt act_dt dve_dt act_chain
        dve_chain dve_parts act_dec pool_wdt act_wdt""".split()
    S = {n: sem(n) for n in names}
    ld_w = [sem(f"ld_w{i}") for i in range(STAGE)]
    ld_wo = [sem(f"ld_wo{i}") for i in range(4)]
    ld_step = [S["ld_step0"], S["ld_step1"]]
    ld_cp = [S["ld_cp0"], S["ld_cp1"]]
    ld_dp = [S["ld_dp0"], S["ld_dp1"]]

    xt = gate[:, 1, :, :]
    wdt_f = yt[:, 0:KD * P]
    wdt_b = mh[:, 0:1, :, :].rearrange("p a h i -> p (a h i)")

    def wdt_part(part, k):
        return wdt_b[:, (part * KD + k) * P:(part * KD + k + 1) * P]

    acs_part = [x2[:, 0, :], x2[:, 1, :], yhl[:, 0, :]]
    b_part = [yhl[:, 1, :], sth[:, 0, :], sth[:, 1, :]]
    def flat(tile):
        return tile.rearrange("p a f -> p (a f)")

    u_t, dt_t = ee[:, :], st[:, :]
    l_t, r_t = flat(mf[:, :, :]), flat(x2f[:, :, :])
    ln_t, a_t = flat(hid[:, 1, 0:2, :]), flat(hid[:, 1, 2:4, :])
    acs_t, bb_t = flat(hid[:, 1, 4:6, :]), flat(hid[:, 1, 6:8, :])

    def splits(c):
        return [(1, j) for j in range(FIRST[c + 1], FIRST[c + 1] + len(PROJ[c + 1]))] if c < CH - 1 else \
               [(2, j) for j in range(len(PROJ[0]))]

    def flags(s):
        if not isinstance(s, int):
            return True, True
        return s + 1 < STEPS, s + 2 < STEPS

    with nc.Block() as block:

        def steps(eng, body):
            body(-1, -1, 1)
            body(0, 0, 0)
            body(1, 0, 1)
            with eng.Fori(1, G - 1) as g:
                body(2 * g, g, 0)
                body(2 * g + 1, g, 1)
            body(STEPS - 2, G - 1, 0)
            body(STEPS - 1, G - 1, 1)

        @block.sync
        def _(sp):
            def load_w(s, g, sg, ahead, j):
                grp = g + (sg + ahead) // 2
                n = NB * (s + ahead) + j
                sp.wait_ge(S["act_Wh"], count(n - STAGE + 1))
                sp.wait_ge(S["pool_Wl"], count(n - STAGE + 1))
                sp.dma_start(wst[:, j % STAGE, :],
                             w_in[bass.ds(grp * NB + j, 1), :, :].rearrange("o p f -> p (o f)")).then_inc(ld_w[j % STAGE], 16)

            def load_mv(s, g, sg, c):
                sp.wait_ge(S["pe_L"], count(16 * s + 4 * c))
                b = sg
                sp.dma_start(mv[48:51, :].rearrange("r (h i) -> r h i", h=HG),
                             acs_dram[:, bass.ds(g * HG, HG), b * TB + c * P:b * TB + (c + 1) * P]).then_inc(S["ld_mv"], 16)

            def load_step(s, g, sg):
                sp.wait_ge(S["pool_Sd"], count(2 * (s - 1)))
                for part in range(3):
                    sp.dma_start(sbt[part * HG:(part + 1) * HG, sg, :],
                                 b_dram[part, bass.ds(g * HG, HG), sg * TB:(sg + 1) * TB]).then_inc(ld_step[sg], 16)
                    sp.dma_start(t48[part * HG:(part + 1) * HG, sg, :],
                                 acs_dram[part, bass.ds(g * HG, HG), sg * TB:(sg + 1) * TB]).then_inc(ld_step[sg], 16)
                src = dec_dram[bass.ds(g * HG, HG), sg * CH:(sg + 1) * CH]
                sp.dma_start(dec[:, sg, :, :], src.unsqueeze(0).broadcast_to([P, HG, CH])).then_inc(ld_step[sg], 16)

            def load_wo(g, half):
                for k in range(4 * half, 4 * half + 4):
                    sp.wait_ge(S["dve_Wo"], count(8 * g + k - 3))
                    sp.wait_ge(S["act_Wo"], count(8 * g + k - 3))
                    sp.dma_start(wost[:, k % 4, :], w_out[bass.ds(g * NPAIR + k, 1), :, :].rearrange("o p f -> p (o f)")
                                 ).then_inc(ld_wo[k % 4], 16)

            def load_dp(s, g, sg):
                sp.wait_ge(S["dve_t2"], count(4 * (s - 1)))
                sp.dma_start(dparam[:, sg, :], dpar[bass.ds(g, 1), :, :].rearrange("o p f -> p (o f)")).then_inc(ld_dp[sg], 16)

            def load_cp(s, g, sg):
                sp.wait_ge(S["dve_conv"], count(NC * (s - 1)))
                sp.dma_start(cparam[:, sg, :, :].rearrange("p a b -> p (a b)"),
                             convp[bass.ds(g, 1), :, :].rearrange("o p f -> p (o f)")).then_inc(ld_cp[sg], 16)

            for i in range(NT):
                sp.dma_start(xt[:, i, :], x[i * P:(i + 1) * P, :]).then_inc(S["ld_x0"] if i < NT // 2 else S["ld_x1"], 16)
            sp.dma_start(small[:, 0:KD], norm_w).then_inc(S["ld_small"], 16)
            sp.dma_start(small[:, KD:KD + 1], dt_bias).then_inc(S["ld_small"], 16)
            sp.dma_start(small[:, KD + 1:KD + 2], a_log).then_inc(S["ld_small"], 16)
            sp.dma_start(wdt_f, w_dt).then_inc(S["ld_wdt"], 16)
            load_cp(0, 0, 0)
            load_dp(0, 0, 0)
            for j in range(STAGE):
                load_w(-1, -1, 1, 1, j)

            def body(s, g, sg):
                proj, split = flags(s)
                ssd = not isinstance(s, int) or s >= 0
                if not ssd:
                    for j in range(STAGE, len(PROJ[0])):
                        load_w(s, g, sg, 1, j)
                for c in range(CH):
                    todo = [(a, j) for a, j in splits(c) if (proj if a == 1 else split)]
                    if c == 1 and ssd and sg == 0:
                        load_wo(g, 1)
                    for a, j in todo[:2]:
                        load_w(s, g, sg, a, j)
                    if ssd and c < CH - 1:
                        load_mv(s, g, sg, c + 1)
                    elif ssd and proj:
                        load_mv(s + 1, g + (sg + 1) // 2, (sg + 1) % 2, 0)
                    for a, j in todo[2:]:
                        load_w(s, g, sg, a, j)
                    if c == 2 and sg == 1 and proj:
                        load_wo(g + 1, 0)
                    if c == 2 and ssd and proj:
                        nsg, ng = (sg + 1) % 2, g + (sg + 1) // 2
                        load_step(s + 1, ng, nsg)
                        load_dp(s + 1, ng, nsg)
                    if not ssd and c == 2:
                        sp.wait_ge(S["dve_parts"], 1)
                        for part in range(3):
                            sp.dma_start(acs_dram[part, :, :], acs_part[part]).then_inc(S["st_scr"], 16)
                        sp.wait_ge(S["act_dec"], 1)
                        sp.dma_start(dec_dram, rs[:, :]).then_inc(S["st_scr"], 16)
                    if not ssd and c == 3:
                        sp.wait_ge(S["dve_parts"], 2)
                        for part in range(3):
                            sp.dma_start(b_dram[part, :, :], b_part[part]).then_inc(S["st_scr"], 16)
                        sp.wait_ge(S["st_scr"], 16 * 7)
                        sp.wait_ge(S["pool_const"], 11)
                        load_step(0, 0, 0)
                        load_mv(0, 0, 0, 0)
                    if c == 3 and split:
                        load_cp(s + 2, g + (sg + 2) // 2, sg)
            steps(sp, body)

        @block.tensor
        def _(pe):
            def three(out_ap, a_hi, a_lo, b_hi, b_lo, first=True, last=True):
                pe.matmul(out_ap, a_hi, b_hi, start=first, stop=False)
                pe.matmul(out_ap, a_hi, b_lo, start=False, stop=False)
                return pe.matmul(out_ap, a_lo, b_hi, start=False, stop=last)

            def proj_block(s, sg, c, i):
                j = FIRST[c] + i
                kind, _ = ORDER[j]
                n = NB * (s + 1) + j
                b = (sg + 1) % 2
                pe.wait_ge(S["act_Wh"], count(n + 1))
                pe.wait_ge(S["pool_Wl"], count(n + 1))
                pk, _ = ORDER[j - 2]
                before = [x[0] != "g" for x in ORDER[:(j - 2) % NB + 1]]
                step_of = s + 1 if j >= 2 else s
                if pk == "g":
                    pe.wait_ge(S["act_gate"], count(NG * step_of + before.count(False)))
                else:
                    pe.wait_ge(S["dve_conv"], count(NC * step_of + before.count(True)))
                o = bP[j % 2][:, :]
                for k in range(KD):
                    mm = three(o, wr[:, 0, j % RING, k * P:(k + 1) * P], wr[:, 1, j % RING, k * P:(k + 1) * P],
                               hT[:, 0, k, b * TB:(b + 1) * TB], hT[:, 1, k, b * TB:(b + 1) * TB],
                               first=(k == 0), last=(k == KD - 1))
                mm.then_inc(S["pe_proj"], 1)

            def decay_logs(s, sg, c, q):
                pe.wait_ge(S["dve_M"], count(16 * s + 4 * c + q - 1))
                pe.matmul(bL[q % 2][:, :], sbt[:, sg, c * P:(c + 1) * P], mv[:, q * 512:(q + 1) * 512],
                          start=True, stop=True).then_inc(S["pe_L"], 1)

            def scores(s, sg, c):
                pe.wait_ge(S["act_BCh"], count(2 * (s + 1)))
                pe.wait_ge(S["pool_BCl"], count(2 * (s + 1)))
                if c > 0:
                    pe.wait_ge(S["dve_S"], count(6 * s + 2 * c))
                else:
                    pe.wait_ge(S["dve_ms"], count(4 * s - 1))
                ck = slice(c * P, (c + 1) * P)
                mm = three(bB[:, 0:P], bc[:, sg, 0, 0, ck], bc[:, sg, 1, 0, ck], bc[:, sg, 0, 1, ck], bc[:, sg, 1, 1, ck])
                for part in range(2 if c < CH - 1 else 0):
                    mm = pe.transpose(bB[:, 256 + 64 * part:256 + 64 * (part + 1)].bitcast(BF16),
                                      bc[:, sg, part, 0, ck], identb[:, :])
                mm.then_inc(S["pe_X"], 1)

            def to_tokens(s, sg, c, half):
                bank = bB if half else bA
                if half == 0:
                    pe.wait_ge(S["act_hs"], count(NC * (s + 1)))
                    if c > 0:
                        pe.wait_ge(S["dve_S"], count(6 * s + 2 * c - 1))
                    else:
                        pe.wait_ge(S["dve_acc"], count(4 * s - 1))
                else:
                    pe.wait_ge(S["dve_CB"], count(4 * s + c + 1))
                    if c < CH - 1:
                        pe.wait_ge(S["act_Bt"], count(3 * s + c + 1))
                for i in range(4):
                    mm = pe.transpose(bank[:, i * P:(i + 1) * P], hid[:, sg, 4 * half + i, c * P:(c + 1) * P], ident[:, :])
                mm.then_inc(S["pe_T"], 1)

            def cumsum_rows(s, sg, c, half):
                pe.wait_ge(S["dve_u"], count(8 * s + 2 * (c - 1) + half + 1))
                for i in range(4):
                    mm = pe.matmul(bD[half][:, i * P:(i + 1) * P], psel[:, 4 * half + i, :], t48[:, sg, c * P:(c + 1) * P],
                                   start=True, stop=True)
                mm.then_inc(S["pe_E"], 1)

            def y_from_state(s, sg, c, half):
                pe.wait_ge(S["act_E"], count(6 * s + 2 * (c - 1) + half + 1))
                pe.wait_ge(S["act_Sh"], count(3 * s + c))
                pe.wait_ge(S["pool_Sl"], count(3 * s + c))
                for i in range(4):
                    pr = 4 * half + i
                    ps, ck = slice(pr * P, (pr + 1) * P), slice(c * P, (c + 1) * P)
                    mm = three(bD[half][:, i * P:(i + 1) * P], sth[:, 0, ps], sth[:, 1, ps],
                               bc[:, sg, 0, 1, ck], bc[:, sg, 1, 1, ck])
                mm.then_inc(S["pe_Yo"], 1)

            def tokens_out(s, c, half):
                pe.wait_ge(S["act_Th"], count(8 * s + 2 * c + half + 1))
                pe.wait_ge(S["dve_Tl"], count(8 * s + 2 * c + half + 1))
                if c < CH - 1:
                    pe.wait_ge(S["dve_X2"], count(6 * s + 2 * c + half + 1))

            def project_out(s, c, fresh=None):
                n = 4 * s + c
                if c < CH:
                    tokens_out(s, c, 0)
                else:
                    pe.wait_ge(S["dve_ms"], count(n - 1))
                    pe.wait_ge(S["dve_acc"], count(n - 1))
                pe.wait_ge(S["act_yh"], count(n))
                pe.wait_ge(S["dve_yl"], count(n))
                for k in range(NPAIR):
                    kp = slice(k * P, (k + 1) * P)
                    if k == 5:
                        if c < CH:
                            tokens_out(s, c, 1)
                        pe.wait_ge(S["pool_ssl"], count(n))
                        for part in range(2):
                            mm = pe.matmul(bB[:, 0:1], ssb[:, part, :], onesb[:, 0:1], start=(part == 0), stop=(part == 1))
                        mm.then_inc(S["pe_ssq"], 1)
                    if fresh is not None:
                        pe.wait_ge(S["act_Wo"], 8 * fresh + k + 1)
                        pe.wait_ge(S["dve_Wo"], 8 * fresh + k + 1)
                    mm = three(bA[:, :], yhl[:, 0, kp], yhl[:, 1, kp], wo[:, 0, k, :], wo[:, 1, k, :],
                               first=(k == 0), last=(k == NPAIR - 1))
                mm.then_inc(S["pe_out"], 1)

            def states(s, c, half):
                if half == 0:
                    pe.wait_ge(S["dve_acc"], count(4 * s + c))
                else:
                    pe.wait_ge(S["dve_ms"], count(4 * s + c))
                if isinstance(s, int) and s == 0 and c == 0:
                    tokens_out(s, c, half)
                pe.wait_ge(S["act_Bt"], count(3 * s + c + 1))
                pe.wait_ge(S["act_X2h"], count(6 * s + 2 * c + half + 1))
                pe.wait_ge(S["pool_X2l"], count(6 * s + 2 * c + half + 1))
                hs = slice(half * 512, (half + 1) * 512)
                three(( bB if half else bA)[:, :], btok[:, 0, :], btok[:, 1, :], x2[:, 0, hs], x2[:, 1, hs]
                      ).then_inc(S["pe_St"], 1)

            def y_diag(s, c, half):
                if c > 0:
                    pe.wait_ge(S["dve_t1"], count(6 * s + 2 * (c - 1) + half + 1))
                else:
                    pe.wait_ge(S["dve_u"], count(8 * s - 1 + half))
                pe.wait_ge(S["dve_Tl"], count(8 * s + 2 * c + half + 1))
                for q in (2 * half, 2 * half + 1):
                    pe.wait_ge(S["act_Mh"], count(16 * s + 4 * c + q + 1))
                    pe.wait_ge(S["pool_Ml"], count(16 * s + 4 * c + q + 1))
                    for i in (2 * (q % 2), 2 * (q % 2) + 1):
                        pr = 4 * half + i
                        o = bD[half][:, i * P:(i + 1) * P]
                        for e in range(2):
                            h = 2 * pr + e
                            mm = three(o, hh[:, 0, 2 * h:2 * h + 2, :], hh[:, 1, 2 * h:2 * h + 2, :],
                                       mh[:, 0, h, :], mh[:, 1, h, :], first=(e == 0), last=(e == 1))
                mm.then_inc(S["pe_Yd"], 1)

            pe.wait_ge(S["pool_ident"], 1)
            for i in range(NT):
                pe.wait_ge(S["dve_xn"], i + 1)
                for k in range(KD):
                    mm = pe.transpose(banks[i][:, k * P:(k + 1) * P], xt[:, i, k * P:(k + 1) * P], ident[:, :])
                mm.then_inc(S["pe_xt"], 1)
            pe.wait_ge(S["act_wdt"], 1)
            pe.wait_ge(S["pool_wdt"], 1)
            pe.wait_ge(S["act_h"], NT)
            pe.wait_ge(S["dve_h"], NT)
            for b in range(2):
                for k in range(KD):
                    mm = three([bA, bB][b][:, :], wdt_part(0, k), wdt_part(1, k), hT[:, 0, k, b * TB:(b + 1) * TB],
                               hT[:, 1, k, b * TB:(b + 1) * TB], first=(k == 0), last=(k == KD - 1))
                mm.then_inc(S["pe_dt"], 1)

            def body(s, g, sg):
                proj, _ = flags(s)
                ssd = not isinstance(s, int) or s >= 0
                prev = not isinstance(s, int) or s > 0
                for c in range(CH):
                    nb = len(PROJ[c])
                    if not ssd:
                        for i in range(nb):
                            proj_block(s, sg, c, i)
                        continue
                    first = isinstance(s, int) and s == 0 and c == 0
                    if first:
                        proj_block(s, sg, c, 0)
                        proj_block(s, sg, c, 1)
                    if c == 0:
                        pe.wait_ge(ld_step[sg], 16 * 7 * (g + 1))
                    pe.wait_ge(S["ld_mv"], 16 * (4 * s + c + 1))
                    decay_logs(s, sg, c, 0)
                    scores(s, sg, c)
                    decay_logs(s, sg, c, 1)
                    to_tokens(s, sg, c, 0)
                    if proj and not first:
                        proj_block(s, sg, c, 0)
                    to_tokens(s, sg, c, 1)
                    if c > 0:
                        cumsum_rows(s, sg, c, 0)
                        cumsum_rows(s, sg, c, 1)
                    decay_logs(s, sg, c, 2)
                    decay_logs(s, sg, c, 3)
                    if proj and not first:
                        proj_block(s, sg, c, 1)
                    if proj:
                        proj_block(s, sg, c, 2)
                    if c > 0:
                        y_from_state(s, sg, c, 0)
                        y_from_state(s, sg, c, 1)
                    if prev or c > 0:
                        project_out(s, c, g if c == 1 and sg == 0 else None)
                    if proj:
                        proj_block(s, sg, c, 3)
                    if proj and nb == 5:
                        proj_block(s, sg, c, 4)
                    if c < CH - 1:
                        states(s, c, 0)
                        states(s, c, 1)
                    y_diag(s, c, 0)
                    y_diag(s, c, 1)
                if isinstance(s, int) and s == STEPS - 1:
                    project_out(s, CH)

            steps(pe, body)

        @block.scalar
        def _(act):
            def split_w(s, ahead, j):
                n = NB * (s + ahead) + j
                act.wait_ge(ld_w[j % STAGE], 16 * ((NB // STAGE) * (s + ahead) + j // STAGE + 1))
                act.wait_ge(S["pe_proj"], count(n - RING + 1))
                act.activation(wr[:, 0, j % RING, :], wst[:, j % STAGE, :], ACT.Copy).then_inc(S["act_Wh"], 1)

            def tap(s, sg, c, i):
                j = FIRST[c] + i
                kind, m = ORDER[j]
                par = (sg + 1) % 2
                x_i = CONV.index((kind, m))
                act.wait_ge(S["pe_proj"], count(NB * (s + 1) + j + 1))
                if kind == "h":
                    act.wait_ge(S["pe_T"], count(8 * s))
                    act.wait_ge(S["dve_t2"], count(4 * s))
                    o = hid[:, par, m, :]
                else:
                    z = 0 if kind == "B" else 1
                    act.wait_ge(S["act_BCh"], count(2 * s + z + 1))
                    act.wait_ge(S["pool_BCl"], count(2 * s + z + 1))
                    o = bctmp[:, z, :]
                act.activation(o, bP[j % 2][:, :], ACT.Identity, bias=cparam[:, par, x_i, 4:5],
                               scale=cparam[:, par, x_i, 3:4]).then_inc(S["act_tap"], 1)

            def silu(s, sg, kind, m):
                par = (sg + 1) % 2
                act.wait_ge(S["dve_conv"], count(NC * (s + 1) + CONV.index((kind, m)) + 1))
                o = hid[:, par, m, :] if kind == "h" else bctmp[:, 0 if kind == "B" else 1, :]
                act.activation(o, o, ACT.Silu).then_inc(S["act_hs"], 1)

            def split_bc(s, sg, kind):
                z = 0 if kind == "B" else 1
                act.wait_ge(S["act_hs"], count(NC * (s + 1) + CONV.index((kind, 0)) + 1))
                act.wait_ge(S["pe_X"], count(4 * s))
                act.wait_ge(S["pe_Yo"], count(6 * s))
                act.activation(bc[:, (sg + 1) % 2, 0, z, :], bctmp[:, z, :], ACT.Copy).then_inc(S["act_BCh"], 1)

            def silu_gate(s, sg, j):
                m = ORDER[j][1]
                act.wait_ge(S["pe_proj"], count(NB * (s + 1) + j + 1))
                act.wait_ge(S["dve_yg"], count(4 * s))
                act.activation(gate[:, (sg + 1) % 2, m, :], bP[j % 2][:, :], ACT.Silu).then_inc(S["act_gate"], 1)

            def decays(s, c, q):
                act.wait_ge(S["pe_L"], count(16 * s + 4 * c + q + 1))
                act.activation(bL[q % 2][:, :], bL[q % 2][:, :], ACT.Exp).then_inc(S["act_L"], 1)

            def m_hi(s, c, q):
                act.wait_ge(S["dve_M"], count(16 * s + 4 * c + q + 1))
                act.wait_ge(S["pe_Yd"], count(8 * s + 2 * c))
                act.activation(mh[:, 0, 4 * q:4 * q + 4, :].rearrange("p h i -> p (h i)"), mf[:, q % 2, :],
                               ACT.Copy).then_inc(S["act_Mh"], 1)

            def y_hi(s, c):
                n = 4 * s + c
                act.wait_ge(S["dve_yg"], count(n))
                act.wait_ge(S["pe_out"], count(n - 1))
                act.activation(yhl[:, 0, :], yt[:, :], ACT.Copy).then_inc(S["act_yh"], 1)

            def y_square(s, c):
                n = 4 * s + c
                act.wait_ge(S["dve_yl"], count(n))
                act.wait_ge(S["act_yh"], count(n))
                act.activation(yt[:, :], yt[:, :], ACT.Square).then_inc(S["act_sq"], 1)

            def b_tok(s, c):
                act.wait_ge(S["dve_CB"], count(4 * s + c + 1))
                act.wait_ge(S["pe_St"], count(6 * s + 2 * c))
                act.activation(btok[:, :, :].rearrange("p a n -> p (a n)"), bB[:, 256:384].bitcast(BF16),
                               ACT.Copy).then_inc(S["act_Bt"], 1)

            def tok_hi(s, c, half):
                act.wait_ge(S["pe_T"], count(8 * s + 2 * c + half + 1))
                act.wait_ge(S["pe_Yd"], count(8 * s + 2 * c))
                src = (bB if half else bA)[:, :].rearrange("p (r e f) -> p r e f", r=4, e=2)
                dst = hh[:, 0, 16 * half:16 * half + 16, :].rearrange("p (r x) f -> p r x f", x=4)[:, :, 0:4:3, :]
                act.activation(dst, src, ACT.Copy).then_inc(S["act_Th"], 1)

            def exp_rows(s, c, half):
                act.wait_ge(S["pe_E"], count(6 * s + 2 * (c - 1) + half + 1))
                act.wait_ge(S["dve_t1"], count(6 * s + 2 * (c - 1)))
                act.activation(ee[:, half * 512:(half + 1) * 512], bD[half][:, :], ACT.Exp
                               ).then_inc(S["act_E"], 1)

            def x2_hi(s, c, half):
                n = 6 * s + 2 * c + half + 1
                act.wait_ge(S["dve_X2"], count(n))
                act.wait_ge(S["pe_St"], count(6 * s + 2 * c))
                act.activation(x2[:, 0, half * 512:(half + 1) * 512], x2f[:, half, :], ACT.Copy).then_inc(S["act_X2h"], 1)

            def state_hi(s, c):
                act.wait_ge(S["dve_S"], count(6 * s + 2 * c + 2))
                act.wait_ge(S["pe_Yo"], count(6 * s + 2 * c))
                act.activation(sth[:, 0, :], st[:, :], ACT.Copy).then_inc(S["act_Sh"], 1)

            def wo_hi(g, k):
                act.wait_ge(ld_wo[k % 4], 16 * (2 * g + k // 4 + 1))
                act.activation(wo[:, 0, k, :], wost[:, k % 4, :], ACT.Copy,
                               scale=dparam[:, 0, NPAIR + k:NPAIR + k + 1]).then_inc(S["act_Wo"], 1)

            for i in range(NT):
                act.wait_ge(S["ld_x0"] if i < NT // 2 else S["ld_x1"], 8 * NT)
                act.activation(yt[:, 512:1024], xt[:, i, :], ACT.Square, accum_out=ms[:, i:i + 1]).then_inc(S["act_sq0"], 1)
                act.wait_ge(S["act_sq0"], i + 1)
            act.wait_ge(S["ld_wdt"], 16)
            act.activation(wdt_b[:, 0:KD * P], wdt_f, ACT.Copy).then_inc(S["act_wdt"], 1)
            for j in range(STAGE):
                split_w(-1, 1, j)
            act.wait_ge(S["dve_hh"], 1)
            act.wait_ge(S["ld_small"], 48)
            for i in range(NT):
                act.wait_ge(S["pe_xt"], i + 1)
                for k in range(KD):
                    ins = act.activation(hT[:, 0, k, i * P:(i + 1) * P], banks[i][:, k * P:(k + 1) * P], ACT.Copy,
                                         scale=small[:, k:k + 1])
                ins.then_inc(S["act_h"], 1)
            ch = [0]

            def link(ins):
                ch[0] += 1
                ins.then_inc(S["act_chain"], 1)
                act.wait_ge(S["act_chain"], ch[0])

            def softplus():
                for b in range(2):
                    act.wait_ge(S["pe_dt"], b + 1)
                    tb = slice(b * TB, (b + 1) * TB)
                    link(act.activation(u_t[:, tb], [bA, bB][b][:, :], ACT.Identity, bias=small[:, KD:KD + 1]))
                    link(act.activation(l_t[:, tb], u_t[:, tb], ACT.Abs))
                    link(act.activation(l_t[:, tb], l_t[:, tb], ACT.Exp, scale=-1.0))
                link(act.activation(small[:, KD + 2:KD + 3], small[:, KD + 1:KD + 2], ACT.Exp))
                act.activation(l_t, l_t, ACT.Ln, bias=1.0).then_inc(S["act_dt"], 1)

            def log_dt():
                act.wait_ge(S["dve_dt"], 1)
                act.activation(ln_t, dt_t, ACT.Ln).then_inc(S["act_dt"], 1)
                act.wait_ge(S["dve_dt"], 2)
                act.activation(rs[:, :], acs_t.rearrange("p (c i) -> p c i", i=P)[:, :, P - 1], ACT.Exp).then_inc(S["act_dec"], 1)

            def body(s, g, sg):
                proj, split = flags(s)
                ssd = not isinstance(s, int) or s >= 0
                prev = not isinstance(s, int) or s > 0
                if proj:
                    act.wait_ge(ld_cp[(sg + 1) % 2], 16 * (g + (sg + 1) // 2 + 1))
                if not ssd:
                    for j in range(STAGE, len(PROJ[0])):
                        split_w(s, 1, j)
                    softplus()
                for c in range(CH):
                    todo = [(a, j) for a, j in splits(c) if (proj if a == 1 else split)]
                    conv = [i for i, x in enumerate(PROJ[c]) if x[0] != "g"] if proj else []
                    gates = [FIRST[c] + i for i, x in enumerate(PROJ[c]) if x[0] == "g"] if proj else []
                    if ssd:
                        decays(s, c, 0)
                        decays(s, c, 1)
                        if c < CH - 1:
                            b_tok(s, c)
                        tok_hi(s, c, 0)
                        if prev or c > 0:
                            y_hi(s, c)
                    if conv:
                        tap(s, sg, c, conv[0])
                    if todo:
                        split_w(s, *todo[0])
                    if ssd:
                        tok_hi(s, c, 1)
                        decays(s, c, 2)
                        decays(s, c, 3)
                        if c > 0:
                            exp_rows(s, c, 0)
                            exp_rows(s, c, 1)
                        if c == 1 and sg == 0:
                            wo_hi(g, 4)
                            wo_hi(g, 5)
                        m_hi(s, c, 0)
                        m_hi(s, c, 1)
                        if prev or c > 0:
                            y_square(s, c)
                    if conv:
                        tap(s, sg, c, conv[1])
                    if ssd:
                        m_hi(s, c, 2)
                        m_hi(s, c, 3)
                        if c == 1 and sg == 0:
                            wo_hi(g, 6)
                            wo_hi(g, 7)
                        if c < CH - 1:
                            x2_hi(s, c, 0)
                            x2_hi(s, c, 1)
                    if len(conv) > 2:
                        tap(s, sg, c, conv[2])
                    for a, j in todo[1:3]:
                        split_w(s, a, j)
                    for i in conv:
                        kind, m = PROJ[c][i]
                        silu(s, sg, kind, m)
                        if kind != "h":
                            split_bc(s, sg, kind)
                    if gates:
                        silu_gate(s, sg, gates[0])
                    if ssd and c == 0 and sg == 0:
                        act.wait_ge(ld_dp[0], 16 * (g + 1))
                        act.wait_ge(S["pe_out"], count(4 * s))
                        for k in range(4):
                            wo_hi(g, k)
                    if ssd and c < CH - 1:
                        state_hi(s, c)
                    for a, j in todo[3:4]:
                        split_w(s, a, j)
                    if gates:
                        silu_gate(s, sg, gates[1])
                    for a, j in todo[4:]:
                        split_w(s, a, j)
                    if not ssd and c == 1:
                        log_dt()
                if isinstance(s, int) and s == STEPS - 1:
                    y_hi(s, CH)
                    y_square(s, CH)

            steps(act, body)

        @block.vector
        def _(dve):
            def conv(s, sg, c, i):
                j = FIRST[c] + i
                kind, m = ORDER[j]
                par = (sg + 1) % 2
                x_i = CONV.index((kind, m))
                o = hid[:, par, m, :] if kind == "h" else bctmp[:, 0 if kind == "B" else 1, :]
                n = NC * (s + 1) + x_i
                dve.wait_ge(S["act_tap"], count(n + 1))
                for d in range(1, 4):
                    if d > 1:
                        dve.wait_ge(S["dve_tap"], 2 * n + d - 1)
                    dve.scalar_tensor_tensor(out=o[:, d:TB], in0=bP[j % 2][:, 0:TB - d], scalar=cparam[:, par, x_i, 3 - d:4 - d],
                                             in1=o[:, d:TB], op0=ALU.mult, op1=ALU.add
                                             ).then_inc(S["dve_tap"] if d < 3 else S["dve_conv"], 1)

            def m_scores(s, c, q):
                n = 16 * s + 4 * c + q
                dve.wait_ge(S["act_L"], count(n + 1))
                if c < CH - 1:
                    if q == 0:
                        dve.wait_ge(S["dve_X2"], count(6 * s + 2 * c))
                    dve.tensor_copy(w16[:, 4 * q:4 * q + 4], bL[q % 2][:, :].rearrange("p (h i) -> p h i", i=P)[:, :, P - 1]
                                ).then_inc(S["dve_w"], 1)
                if q == 0:
                    dve.wait_ge(S["dve_CB"], 4 * s + c + 1)
                dve.wait_ge(S["act_Mh"], count(n - 1))
                dve.wait_ge(S["pool_Ml"], count(n - 1))
                dve.scalar_tensor_tensor(out=mf[:, q % 2, :].rearrange("p (h i) -> p h i", i=P),
                                         in0=bL[q % 2][:, :].rearrange("p (h i) -> p h i", i=P), scalar=BIG,
                                         in1=cbm[:, :].unsqueeze(1).to_broadcast([P, 4, P]), op0=ALU.min, op1=ALU.mult
                                         ).then_inc(S["dve_M"], 1)

            def y_sum(s, c):
                n = 4 * s + c
                dve.wait_ge(S["dve_t2"], count(n))
                for half in range(2):
                    hs = slice(half * 512, (half + 1) * 512)
                    dve.wait_ge(S["pe_Yd"], count(2 * n - 1 + half))
                    dve.tensor_tensor(yt[:, hs], bD[half][:, :], yt[:, hs], ALU.add).then_inc(S["dve_u"], 1)

            def y_gate(s, c, par, pc):
                if c < CH:
                    dve.wait_ge(S["act_gate"], count(NG * s if c == 0 else NG * (s + 1)))
                dve.wait_ge(S["dve_u"], count(2 * (4 * s + c)))
                v = yt[:, :].rearrange("p (r i) -> p r i", i=P)
                dve.tensor_tensor(v, v, gate[:, par, :, pc * P:(pc + 1) * P], ALU.mult).then_inc(S["dve_yg"], 1)

            def y_lo(s, c):
                n = 4 * s + c
                dve.wait_ge(S["act_yh"], count(n))
                dve.tensor_tensor(yhl[:, 1, :], yt[:, :], yhl[:, 0, :], ALU.subtract).then_inc(S["dve_yl"], 1)

            def masked(s, c):
                dve.wait_ge(S["pe_X"], count(4 * s + c + 1))
                dve.wait_ge(S["dve_M"], count(16 * s + 4 * c))
                dve.tensor_tensor(cbm[:, :], bB[:, 0:P], mask[:, :], ALU.mult).then_inc(S["dve_CB"], 1)

            def tok_lo(s, c, half):
                n = 8 * s + 2 * c + half + 1
                dve.wait_ge(S["act_Th"], count(n))
                src = (bB if half else bA)[:, :].rearrange("p (r e f) -> p r e f", r=4, e=2)
                sel = [hh[:, z, 16 * half:16 * half + 16, :].rearrange("p (r x) f -> p r x f", x=4)[:, :, 0:4:3, :]
                       for z in range(2)]
                dve.tensor_tensor(sel[1], src, sel[0], ALU.subtract).then_inc(S["dve_Tl"], 1)

            def decayed(s, c, half):
                n = 6 * s + 2 * c + half + 1
                dve.wait_ge(S["dve_w"], 12 * s + 4 * c + 2 * half + 2)
                dve.wait_ge(S["act_X2h"], count(n - 2))
                dve.wait_ge(S["pool_X2l"], count(n - 2))
                dve.tensor_tensor(x2f[:, half, :].rearrange("p (h f) -> p h f", f=HP),
                                  (bB if half else bA)[:, :].rearrange("p (h f) -> p h f", f=HP),
                                  w16[:, 8 * half:8 * half + 8].unsqueeze(2).to_broadcast([P, 8, HP]), ALU.mult
                                  ).then_inc(S["dve_X2"], 1)

            def mean_square(s, c):
                n = 4 * s + c
                dve.wait_ge(S["pe_ssq"], count(n))
                dve.wait_ge(S["pool_r"], count(n - 1))
                dve.tensor_scalar(ms[:, 0:1], bB[:, 0:1], 1.0 / GC, EPS, ALU.mult, ALU.add).then_inc(S["dve_ms"], 1)

            def y_start(s, sg, c, done):
                n = 4 * s + c
                dve.wait_ge(S["pool_ssl"], count(n))
                if c > 0:
                    for half in range(2):
                        hs = slice(half * 512, (half + 1) * 512)
                        dve.wait_ge(S["pe_Yo"], count(6 * s + 2 * (c - 1) + half + 1))
                        dve.wait_ge(S["act_E"], count(6 * s + 2 * (c - 1) + half + 1))
                        dve.tensor_tensor(yt[:, hs], bD[half][:, :], ee[:, hs], ALU.mult).then_inc(S["dve_t1"], 1)
                for r in range(NPAIR):
                    if r == NPAIR // 2 and done:
                        mean_square(s, c)
                    rs_ = slice(r * P, (r + 1) * P)
                    hv = hid[:, sg, r, c * P:(c + 1) * P]
                    if c > 0:
                        if r % 4 == 0:
                            dve.wait_ge(S["dve_t1"], count(6 * s + 2 * (c - 1) + r // 4 + 1))
                        ins = dve.scalar_tensor_tensor(out=yt[:, rs_], in0=hv, scalar=dparam[:, sg, r:r + 1], in1=yt[:, rs_],
                                                       op0=ALU.mult, op1=ALU.add)
                    else:
                        ins = dve.tensor_scalar(yt[:, rs_], hv, dparam[:, sg, r:r + 1], None, ALU.mult)
                ins.then_inc(S["dve_t2"], 1)

            def add_out(s, c, blk):
                n = 4 * s + c
                dve.wait_ge(S["pe_out"], count(n))
                dve.wait_ge(S["pool_r"], count(n))
                dve.wait_ge(S["dve_acc"], count(n - 1))
                dve.scalar_tensor_tensor(out=acc[:, blk, :], in0=bA[:, :], scalar=rs[:, 0:1], in1=acc[:, blk, :],
                                         op0=ALU.mult, op1=ALU.add).then_inc(S["dve_acc"], 1)

            def norm_stats(i):
                dve.wait_ge(S["dve_acc"], 4 * (STEPS - 1) + max(i - CH + 1, 0))
                dve.bn_stats(stat[:, i, :], acc[:, i, :]).then_inc(S["dve_st"], 1)
                dve.wait_ge(S["dve_st"], 2 * i + 1)
                dve.bn_aggr(mvar[:, i, :], stat[:, i, :]).then_inc(S["dve_st"], 1)

            def state_add(s, c):
                if c == 0:
                    dve.wait_ge(S["act_Sh"], count(3 * s))
                    dve.wait_ge(S["pool_Sl"], count(3 * s))
                else:
                    dve.wait_ge(S["pool_Sd"], count(2 * s + c))
                for half in range(2):
                    hs = slice(half * 512, (half + 1) * 512)
                    bank = bB if half else bA
                    dve.wait_ge(S["pe_St"], count(6 * s + 2 * c + half + 1))
                    if c == 0:
                        dve.tensor_copy(st[:, hs], bank[:, :]).then_inc(S["dve_S"], 1)
                    else:
                        dve.tensor_tensor(st[:, hs], bank[:, :], st[:, hs], ALU.add).then_inc(S["dve_S"], 1)

            def wo_lo(g, k):
                dve.wait_ge(S["act_Wo"], 8 * g + k + 1)
                dve.scalar_tensor_tensor(out=wo[:, 1, k, :], in0=wost[:, k % 4, :], scalar=dparam[:, 0, NPAIR + k:NPAIR + k + 1],
                                         in1=wo[:, 0, k, :], op0=ALU.mult, op1=ALU.subtract).then_inc(S["dve_Wo"], 1)

            for i in range(NT):
                dve.wait_ge(S["ld_x0"] if i < NT // 2 else S["ld_x1"], 8 * NT)
                dve.tensor_scalar(acc[:, i, :], xt[:, i, :], 2.0, None, ALU.mult).then_inc(S["dve_x2"], 1)
            dve.memset(hh[:, :, :, :], 0.0).then_inc(S["dve_hh"], 1)
            dve.wait_ge(S["act_sq0"], NT)
            dve.tensor_scalar(ms[:, :], ms[:, :], 1.0 / D, EPS, ALU.mult, ALU.add).then_inc(S["dve_ms0"], 1)
            dve.wait_ge(S["pool_rs0"], 1)
            dve.wait_ge(S["dve_x2"], NT)
            for i in range(NT):
                dve.tensor_scalar(xt[:, i, :], xt[:, i, :], rs[:, i:i + 1], None, ALU.mult).then_inc(S["dve_xn"], 1)
            dve.wait_ge(S["ld_small"], 48)
            for i in range(NT):
                dve.wait_ge(S["act_h"], i + 1)
                for k in range(KD):
                    ins = dve.scalar_tensor_tensor(out=hT[:, 1, k, i * P:(i + 1) * P], in0=banks[i][:, k * P:(k + 1) * P],
                                                   scalar=small[:, k:k + 1], in1=hT[:, 0, k, i * P:(i + 1) * P],
                                                   op0=ALU.mult, op1=ALU.subtract)
                ins.then_inc(S["dve_h"], 1)
            ch = [0]

            def link(ins):
                ch[0] += 1
                ins.then_inc(S["dve_chain"], 1)
                dve.wait_ge(S["dve_chain"], ch[0])

            def cumsums():
                dve.wait_ge(S["act_dt"], 1)
                link(dve.scalar_tensor_tensor(out=dt_t, in0=u_t, scalar=0.0, in1=l_t, op0=ALU.max, op1=ALU.add))
                link(dve.tensor_scalar(small[:, KD + 3:KD + 4], small[:, KD + 2:KD + 3], -1.0, None, ALU.mult))
                dve.tensor_scalar(dt_t, dt_t, TINY, None, ALU.max).then_inc(S["dve_dt"], 1)
                dve.wait_ge(S["dve_dt"], 1)
                link(dve.tensor_scalar(a_t, dt_t, small[:, KD + 3:KD + 4], None, ALU.mult))
                link(dve.memset(u_t, 1.0))
                for i in range(NT):
                    ins = dve.tensor_tensor_scan(out=acs_t[:, i * P:(i + 1) * P], data0=u_t[:, i * P:(i + 1) * P],
                                                 data1=a_t[:, i * P:(i + 1) * P], initial=0.0, op0=ALU.mult, op1=ALU.add)
                ins.then_inc(S["dve_dt"], 1)

            def cumsum_parts(src, parts):
                dve.wait_ge(S["dve_dt"], 2)
                link(dve.tensor_copy(parts[0], src))
                link(dve.tensor_tensor(r_t, src, parts[0], ALU.subtract))
                link(dve.tensor_copy(parts[1], r_t))
                dve.tensor_tensor(parts[2], r_t, parts[1], ALU.subtract).then_inc(S["dve_parts"], 1)
                dve.wait_ge(S["dve_parts"], 1)

            def body(s, g, sg):
                proj, _ = flags(s)
                ssd = not isinstance(s, int) or s >= 0
                prev = not isinstance(s, int) or s > 0
                for c in range(CH):
                    cv = [i for i, x in enumerate(PROJ[c]) if x[0] != "g"] if proj else []
                    if proj and c == 0:
                        dve.wait_ge(ld_cp[(sg + 1) % 2], 16 * (g + (sg + 1) // 2 + 1))
                    if not ssd:
                        for i in cv:
                            conv(s, sg, c, i)
                        if c == 0:
                            cumsums()
                        if c == 1:
                            cumsum_parts(acs_t, acs_part)
                        if c == 2:
                            dve.wait_ge(S["act_dt"], 2)
                            link(dve.tensor_tensor(bb_t, acs_t, ln_t, ALU.subtract))
                            cumsum_parts(bb_t, b_part)
                        continue
                    done = prev or c > 0
                    if done:
                        y_sum(s, c)
                    masked(s, c)
                    if done:
                        y_gate(s, c, (sg - 1) % 2 if c == 0 else sg, (c - 1) % CH)
                    m_scores(s, c, 0)
                    m_scores(s, c, 1)
                    tok_lo(s, c, 0)
                    if done:
                        y_lo(s, c)
                    if cv:
                        conv(s, sg, c, cv[0])
                    tok_lo(s, c, 1)
                    if c < CH - 1:
                        decayed(s, c, 0)
                    if c == 1 and sg == 0:
                        wo_lo(g, 4)
                        wo_lo(g, 5)
                    m_scores(s, c, 2)
                    m_scores(s, c, 3)
                    if c < CH - 1:
                        decayed(s, c, 1)
                    if cv:
                        conv(s, sg, c, cv[1])
                    if c == 1 and sg == 0:
                        wo_lo(g, 6)
                        wo_lo(g, 7)
                    if c == 0:
                        dve.wait_ge(ld_dp[sg], 16 * (g + 1))
                    if len(cv) > 2:
                        conv(s, sg, c, cv[2])
                    y_start(s, sg, c, done)
                    if done:
                        add_out(s, c, ((sg - 1) % 2) * CH + CH - 1 if c == 0 else sg * CH + c - 1)
                    if isinstance(s, int) and s == STEPS - 1:
                        for i in (range(CH) if c == 0 else [CH + c - 1]):
                            norm_stats(i)
                    if c == 0 and sg == 0:
                        for k in range(3):
                            wo_lo(g, k)
                    if c < CH - 1:
                        state_add(s, c)
                    if c == 0 and sg == 0:
                        wo_lo(g, 3)
                if isinstance(s, int) and s == STEPS - 1:
                    y_sum(s, CH)
                    y_gate(s, CH, sg, CH - 1)
                    y_lo(s, CH)
                    mean_square(s, CH)
                    add_out(s, CH, sg * CH + CH - 1)

            steps(dve, body)

        @block.gpsimd
        def _(pool):
            def split_w(s, ahead, j):
                n = NB * (s + ahead) + j
                pool.wait_ge(S["act_Wh"], count(n + 1))
                pool.wait_ge(S["pe_proj"], count(n - RING + 1))
                pool.tensor_tensor(wr[:, 1, j % RING, :], wst[:, j % STAGE, :], wr[:, 0, j % RING, :], ALU.subtract
                                   ).then_inc(S["pool_Wl"], 1)

            def m_lo(s, c, q):
                n = 16 * s + 4 * c + q + 1
                pool.wait_ge(S["act_Mh"], count(n))
                pool.tensor_tensor(mh[:, 1, 4 * q:4 * q + 4, :].rearrange("p h i -> p (h i)"), mf[:, q % 2, :],
                                   mh[:, 0, 4 * q:4 * q + 4, :].rearrange("p h i -> p (h i)"), ALU.subtract
                                   ).then_inc(S["pool_Ml"], 1)

            def sum_squares(s, c):
                n = 4 * s + c
                pool.wait_ge(S["act_sq"], count(n))
                for i, w in enumerate((512, 256)):
                    pool.tensor_tensor(yt[:, 0:w], yt[:, 0:w], yt[:, w:2 * w], ALU.add).then_inc(S["pool_sum"], 1)
                    pool.wait_ge(S["pool_sum"], count(4 * (n - 1) + i + 1))
                pool.wait_ge(S["pe_ssq"], count(n - 1))
                pool.tensor_tensor(ssb[:, 0, :], yt[:, 0:P], yt[:, P:2 * P], ALU.add).then_inc(S["pool_sum"], 1)
                pool.wait_ge(S["pool_sum"], count(4 * (n - 1) + 3))
                pool.tensor_tensor(yt[:, 0:P], yt[:, 0:P], yt[:, P:2 * P], ALU.add).then_inc(S["pool_sum"], 1)
                pool.wait_ge(S["pool_sum"], count(4 * n))
                pool.tensor_tensor(ssb[:, 1, :], yt[:, 0:P], ssb[:, 0, :], ALU.subtract).then_inc(S["pool_ssl"], 1)

            def x2_lo(s, c, half):
                n = 6 * s + 2 * c + half + 1
                hs = slice(half * 512, (half + 1) * 512)
                pool.wait_ge(S["act_X2h"], count(n))
                pool.tensor_tensor(x2[:, 1, hs], x2f[:, half, :], x2[:, 0, hs], ALU.subtract).then_inc(S["pool_X2l"], 1)

            def decay_state(s, g, sg, c):
                pool.wait_ge(S["act_Sh"], count(3 * s + c))
                pool.wait_ge(S["pool_Sl"], count(3 * s + c))
                if c == 1:
                    pool.wait_ge(ld_step[sg], 16 * 7 * (g + 1))
                v = st[:, :].rearrange("p (h f) -> p h f", f=HP)
                pool.tensor_tensor(v, v, dec[:, sg, :, c].unsqueeze(2).to_broadcast([P, HG, HP]), ALU.mult
                                   ).then_inc(S["pool_Sd"], 1)

            def rstd(s, c):
                n = 4 * s + c
                pool.wait_ge(S["dve_ms"], count(n))
                pool.wait_ge(S["dve_acc"], count(n - 1))
                pool.tensor_tensor(rs[:, 0:1], ms[:, 0:1], mhalf[:, 0:1], ALU.pow).then_inc(S["pool_r"], 1)

            def state_lo(s, c):
                pool.wait_ge(S["act_Sh"], count(3 * s + c + 1))
                pool.tensor_tensor(sth[:, 1, :], st[:, :], sth[:, 0, :], ALU.subtract).then_inc(S["pool_Sl"], 1)

            def split_bc(s, sg, kind):
                z = 0 if kind == "B" else 1
                pool.wait_ge(S["act_BCh"], count(2 * (s + 1) + z + 1))
                par = (sg + 1) % 2
                pool.tensor_tensor(bc[:, par, 1, z, :], bctmp[:, z, :], bc[:, par, 0, z, :], ALU.subtract
                                   ).then_inc(S["pool_BCl"], 1)

            pool.memset(ident[:, :], 0.0).then_inc(S["pool_fill"], 1)
            pool.memset(mhalf[:, :], -0.5).then_inc(S["pool_fill"], 1)
            pool.wait_ge(S["pool_fill"], 2)
            pool.affine_select(out=ident[:, :], in_=ident[:, :], compare_op=ALU.not_equal, fill=1.0, base=0,
                               pattern=[[-1, P]], channel_multiplier=1).then_inc(S["pool_ident"], 1)
            pool.memset(sbt[:, :, :], 0.0).then_inc(S["pool_fill"], 1)
            pool.memset(mv[:, :], 0.0).then_inc(S["pool_fill"], 1)
            pool.memset(psel[:, :, :], 0.0).then_inc(S["pool_fill"], 1)
            pool.memset(mask[:, :], 1.0).then_inc(S["pool_fill"], 1)
            pool.memset(onesb[:, :], 1.0).then_inc(S["pool_fill"], 1)
            pool.wait_ge(S["pool_fill"], 7)
            pool.wait_ge(S["pool_ident"], 1)
            pool.memset(sbt[0:64, :, :], 1.0).then_inc(S["pool_const"], 1)
            pool.wait_ge(S["pool_const"], 1)
            pool.affine_select(out=mask[:, :], in_=mask[:, :], compare_op=ALU.is_ge, fill=0.0, base=0,
                               pattern=[[1, P]], channel_multiplier=-1).then_inc(S["pool_const"], 1)
            pool.tensor_copy(identb[:, :], ident[:, :]).then_inc(S["pool_const"], 1)
            pool.wait_ge(S["dve_ms0"], 1)
            pool.tensor_tensor(rs[:, :], ms[:, :], mhalf[:, :], ALU.pow).then_inc(S["pool_rs0"], 1)
            pool.wait_ge(S["act_wdt"], 1)
            pool.tensor_tensor(wdt_b[:, KD * P:2 * KD * P], wdt_f, wdt_b[:, 0:KD * P], ALU.subtract).then_inc(S["pool_wdt"], 1)
            for j in range(STAGE):
                split_w(-1, 1, j)
            pool.wait_ge(S["pool_const"], 3)
            pool.wait_ge(S["pool_Wl"], STAGE)
            pairs = sbt[64:P, :, :].rearrange("r a (c n e) -> r (a c) n e", e=2, n=P // 2)
            pool.affine_select(out=pairs, in_=pairs, compare_op=ALU.not_equal, fill=1.0, base=1,
                               pattern=[[0, 2 * CH], [-1, P // 2], [0, 2]], channel_multiplier=1).then_inc(S["pool_const"], 1)
            pool.wait_ge(S["pool_const"], 4)
            before = mv[64:P, :].rearrange("r (h i) -> r h i", i=P)
            pool.affine_select(out=before, in_=before, compare_op=ALU.is_ge, fill=ABOVE, base=-2,
                               pattern=[[0, HG], [1, P]], channel_multiplier=-2).then_inc(S["pool_const"], 1)
            for part in range(3):
                pool.wait_ge(S["pool_const"], 5 + 2 * part)
                rows = mv[0:48, :].rearrange("r (h i) -> r h i", i=P)
                pool.affine_select(out=rows, in_=rows, compare_op=ALU.not_equal, fill=-1.0, base=-HG * part,
                                   pattern=[[-1, HG], [0, P]], channel_multiplier=1).then_inc(S["pool_const"], 1)
                pool.wait_ge(S["pool_const"], 6 + 2 * part)
                rows = psel[:, :, :].rearrange("r a (e f) -> r a e f", e=2)
                pool.affine_select(out=rows, in_=rows, compare_op=ALU.not_equal, fill=1.0, base=-HG * part,
                                   pattern=[[-2, NPAIR], [-1, 2], [0, HP]], channel_multiplier=1).then_inc(S["pool_const"], 1)
            def body(s, g, sg):
                proj, split = flags(s)
                ssd = not isinstance(s, int) or s >= 0
                prev = not isinstance(s, int) or s > 0
                if not ssd:
                    for j in range(STAGE, len(PROJ[0])):
                        split_w(s, 1, j)
                    pool.wait_ge(S["pool_const"], 11)
                for c in range(CH):
                    todo = [(a, j) for a, j in splits(c) if (proj if a == 1 else split)]
                    bcs = [x[0] for x in PROJ[c] if x[0] in "BC"] if proj else []
                    if todo:
                        split_w(s, *todo[0])
                    if ssd:
                        m_lo(s, c, 0)
                        m_lo(s, c, 1)
                        if prev or c > 0:
                            sum_squares(s, c)
                        m_lo(s, c, 2)
                        m_lo(s, c, 3)
                        if c < CH - 1:
                            x2_lo(s, c, 0)
                            x2_lo(s, c, 1)
                        if (prev or c > 0) and c < CH - 1:
                            rstd(s, c)
                        if 0 < c < CH - 1:
                            decay_state(s, g, sg, c)
                    for a, j in todo[1:2]:
                        split_w(s, a, j)
                    if ssd and c == CH - 1:
                        rstd(s, c)
                    for a, j in todo[2:3]:
                        split_w(s, a, j)
                    for kind in bcs:
                        split_bc(s, sg, kind)
                    if ssd and c < CH - 1:
                        state_lo(s, c)
                    for a, j in todo[3:]:
                        split_w(s, a, j)
                if isinstance(s, int) and s == STEPS - 1:
                    sum_squares(s, CH)
                    rstd(s, CH)

            steps(pool, body)


def ffn(nc, ctx, banks, acc, ident, stat, mvar, wgu, zgu, sgu, wdn, zdn, sdn, out):
    def sb(name, shape, dt=F32):
        return ctx.enter_context(nc.sbuf_tensor(name, shape, dt))

    def sem(name):
        return ctx.enter_context(nc.semaphore(name))

    GU = 2 * KD * P
    yout = sb("f_y", [P, NT, D])
    x1T = sb("f_x1T", [P, 2, KD, T], BF16)
    gq = sb("f_gq", [P, 2, GU], I32)
    gz = sb("f_gz", [P, 2, GU], I32)
    gs = sb("f_gs", [P, 2, GU])
    gw = sb("f_gw", [P, 2, GU])
    gh = sb("f_gh", [P, 2, 2, GU], BF16)
    dq = sb("f_dq", [P, 2, D], I32)
    dz = sb("f_dz", [P, 2, D], I32)
    ds_ = sb("f_ds", [P, 2, D])
    dw = sb("f_dw", [P, 2, D])
    dh = sb("f_dh", [P, 2, NF, D], BF16)
    sg = sb("f_sg", [P, 2, TB])
    hf = sb("f_hf", [P, 2, NF, T], BF16)
    rstd = sb("f_rstd", [P, NT])
    mh = sb("f_mhalf", [P, NT])

    names = """pool_c dve_st dve_ag dve_ve pool_r dve_x1 pe_t act_t dve_t
        dve_gq dve_gs act_gh pool_gl dve_dq dve_ds act_dh pool_dl pe_g pe_u act_sg dve_h act_hh pool_hl
        pe_d dve_z2 dve_st2 dve_ag2 dve_ve2 pool_r2 dve_y""".split()
    S = {n: sem("f_" + n) for n in names}
    ld_g = [sem(f"f_ld_g{i}") for i in range(2)]
    ld_d = [sem(f"f_ld_d{i}") for i in range(2)]
    st_y = sem("f_st_y")

    with nc.Block() as block:

        def blocks(eng, body):
            body(0, 0)
            body(1, 1)
            with eng.Fori(1, NF // 2 - 1) as i:
                body(2 * i, 0)
                body(2 * i + 1, 1)
            body(NF - 2, 0)
            body(NF - 1, 1)

        @block.sync
        def _(sp):
            def body(f, e):
                sp.wait_ge(S["dve_gs"], count(f - 1))
                o = bass.ds(f, 1)
                sp.dma_start(gq[:, e, :], wgu[o, :, :].rearrange("o p f -> p (o f)")).then_inc(ld_g[e], 16)
                sp.dma_start(gz[:, e, :], zgu[o, :].broadcast_to([P, GU])).then_inc(ld_g[e], 16)
                sp.dma_start(gs[:, e, :], sgu[o, :].broadcast_to([P, GU])).then_inc(ld_g[e], 16)
                sp.wait_ge(S["dve_ds"], count(f - 1))
                sp.dma_start(dq[:, e, :], wdn[o, :, :].rearrange("o p f -> p (o f)")).then_inc(ld_d[e], 16)
                sp.dma_start(dz[:, e, :], zdn[o, :].broadcast_to([P, D])).then_inc(ld_d[e], 16)
                sp.dma_start(ds_[:, e, :], sdn[o, :].broadcast_to([P, D])).then_inc(ld_d[e], 16)

            blocks(sp, body)
            for i in range(NT):
                sp.wait_ge(S["dve_y"], i + 1)
                sp.dma_start(out[i * P:(i + 1) * P, :], yout[:, i, :]).then_inc(st_y, 16)
            sp.wait_ge(st_y, 16 * NT)

        @block.tensor
        def _(pe):
            def three(out_ap, a_hi, a_lo, b_hi, b_lo, first=True, last=True):
                pe.matmul(out_ap, a_hi, b_hi, start=first, stop=False)
                pe.matmul(out_ap, a_hi, b_lo, start=False, stop=False)
                return pe.matmul(out_ap, a_lo, b_hi, start=False, stop=last)

            for i in range(NT):
                pe.wait_ge(S["dve_x1"], i + 1)
                for k in range(KD):
                    mm = pe.transpose(banks[i][:, k * P:(k + 1) * P], acc[:, i, k * P:(k + 1) * P], ident[:, :])
                mm.then_inc(S["pe_t"], 1)

            def body(f, e):
                pe.wait_ge(S["act_gh"], count(f + 1))
                pe.wait_ge(S["pool_gl"], count(f + 1))
                pe.wait_ge(S["act_sg"], count(2 * f - 2))
                pe.wait_ge(S["dve_h"], count(2 * f - 2))
                for u in range(2):
                    for half in range(2):
                        if isinstance(f, int) and f == 0:
                            pe.wait_ge(S["act_t"], (half + 1) * NT // 2)
                            pe.wait_ge(S["dve_t"], (half + 1) * NT // 2)
                        for k in range(KD):
                            w = slice((u * KD + k) * P, (u * KD + k + 1) * P)
                            ts = slice(half * TB, (half + 1) * TB)
                            mm = three(banks[4 * e + 2 * u + half][:, :], gh[:, 0, e, w], gh[:, 1, e, w],
                                       x1T[:, 0, k, ts], x1T[:, 1, k, ts], first=(k == 0), last=(k == KD - 1))
                        mm.then_inc(S["pe_u"] if u else S["pe_g"], 1)

            blocks(pe, body)
            pe.wait_ge(S["act_hh"], 2 * NF - 2)
            pe.wait_ge(S["pool_hl"], 2 * NF - 2)
            pe.wait_ge(S["act_dh"], NF)
            pe.wait_ge(S["pool_dl"], NF)
            for i in range(NT):
                tk = slice(i * P, (i + 1) * P)
                for f in range(NF):
                    if i == 0 and f == NF - 1:
                        pe.wait_ge(S["act_hh"], 2 * NF)
                        pe.wait_ge(S["pool_hl"], 2 * NF)
                    mm = three(banks[i][:, :], hf[:, 0, f, tk], hf[:, 1, f, tk], dh[:, 0, f, :], dh[:, 1, f, :],
                               first=(f == 0), last=(f == NF - 1))
                mm.then_inc(S["pe_d"], 1)

        @block.scalar
        def _(act):
            def split(f, e):
                act.wait_ge(S["dve_gs"], count(f + 1))
                act.wait_ge(S["pe_u"], count(2 * f - 2))
                act.activation(gh[:, 0, e, :], gw[:, e, :], ACT.Copy).then_inc(S["act_gh"], 1)
                act.wait_ge(S["dve_ds"], count(f + 1))
                act.activation(dh[:, 0, bass.ds(f, 1), :], dw[:, e, :].unsqueeze(1), ACT.Copy).then_inc(S["act_dh"], 1)

            for i in range(NT):
                act.wait_ge(S["pe_t"], i + 1)
                act.activation(x1T[:, 0, :, i * P:(i + 1) * P], banks[i][:, :].rearrange("p (k t) -> p k t", t=P),
                               ACT.Copy).then_inc(S["act_t"], 1)
            split(0, 0)

            def body(f, e):
                if not isinstance(f, int) or f + 1 < NF:
                    split(f + 1, 1 - e)
                for half in range(2):
                    act.wait_ge(S["pe_g"], count(2 * f + half + 1))
                    act.wait_ge(S["act_hh"], count(2 * f + half - 1))
                    act.wait_ge(S["pool_hl"], count(2 * f + half - 1))
                    act.activation(sg[:, half, :], banks[4 * e + half][:, :], ACT.Silu).then_inc(S["act_sg"], 1)
                for half in range(2):
                    act.wait_ge(S["dve_h"], count(2 * f + half + 1))
                    act.activation(hf[:, 0, bass.ds(f, 1), half * TB:(half + 1) * TB], sg[:, half, :].unsqueeze(1),
                                   ACT.Copy).then_inc(S["act_hh"], 1)

            blocks(act, body)

        @block.vector
        def _(dve):
            def dequant_gate_up(f, e):
                dve.wait_ge(ld_g[e], 24 * (f - e) + 48)
                dve.wait_ge(S["act_gh"], count(f - 1))
                dve.wait_ge(S["pool_gl"], count(f - 1))
                dve.tensor_tensor(gw[:, e, :], gq[:, e, :], gz[:, e, :], ALU.subtract).then_inc(S["dve_gq"], 1)
                dve.wait_ge(S["dve_gq"], f + 1)
                dve.tensor_tensor(gw[:, e, :], gw[:, e, :], gs[:, e, :], ALU.mult).then_inc(S["dve_gs"], 1)

            def dequant_down(f, e):
                dve.wait_ge(ld_d[e], 24 * (f - e) + 48)
                dve.wait_ge(S["act_dh"], count(f - 1))
                dve.wait_ge(S["pool_dl"], count(f - 1))
                dve.tensor_tensor(dw[:, e, :], dq[:, e, :], dz[:, e, :], ALU.subtract).then_inc(S["dve_dq"], 1)
                dve.wait_ge(S["dve_dq"], f + 1)
                dve.tensor_tensor(dw[:, e, :], dw[:, e, :], ds_[:, e, :], ALU.mult).then_inc(S["dve_ds"], 1)

            dve.bn_stats(stat[:, NT - 1, :], acc[:, NT - 1, :]).then_inc(S["dve_st"], 1)
            dve.wait_ge(S["dve_st"], 1)
            dve.bn_aggr(mvar[:, NT - 1, :], stat[:, NT - 1, :]).then_inc(S["dve_ag"], 1)
            dve.wait_ge(S["dve_ag"], 1)
            dve.tensor_scalar(rstd[:, :], mvar[:, :, 1], EPS, None, ALU.add).then_inc(S["dve_ve"], 1)
            dve.wait_ge(S["pool_r"], 1)
            for i in range(NT):
                dve.tensor_scalar(acc[:, i, :], acc[:, i, :], mvar[:, i, 0:1], rstd[:, i:i + 1], ALU.subtract, ALU.mult
                                  ).then_inc(S["dve_x1"], 1)
            dequant_gate_up(0, 0)
            for i in range(NT):
                dve.wait_ge(S["act_t"], i + 1)
                tk = slice(i * P, (i + 1) * P)
                dve.tensor_tensor(x1T[:, 1, :, tk], banks[i][:, :].rearrange("p (k t) -> p k t", t=P), x1T[:, 0, :, tk],
                                  ALU.subtract).then_inc(S["dve_t"], 1)
            dequant_down(0, 0)
            dequant_gate_up(1, 1)
            dequant_down(1, 1)

            def body(f, e):
                for half in range(2):
                    dve.wait_ge(S["pe_u"], 2 * f + half + 1)
                    dve.wait_ge(S["act_sg"], 2 * f + half + 1)
                    dve.tensor_tensor(sg[:, half, :], banks[4 * e + 2 + half][:, :], sg[:, half, :], ALU.mult
                                      ).then_inc(S["dve_h"], 1)
                if not isinstance(f, int) or f + 2 < NF:
                    dequant_gate_up(f + 2, e)
                    dequant_down(f + 2, e)

            blocks(dve, body)
            for i in range(NT):
                dve.wait_ge(S["pe_d"], i + 1)
                dve.tensor_tensor(yout[:, i, :], banks[i][:, :], acc[:, i, :], ALU.add).then_inc(S["dve_z2"], 1)
                dve.wait_ge(S["dve_z2"], i + 1)
                dve.bn_stats(stat[:, i, :], yout[:, i, :]).then_inc(S["dve_st2"], 1)
                dve.wait_ge(S["dve_st2"], i + 1)
                dve.bn_aggr(mvar[:, i, :], stat[:, i, :]).then_inc(S["dve_ag2"], 1)
                dve.wait_ge(S["dve_ag2"], i + 1)
                dve.tensor_scalar(rstd[:, i:i + 1], mvar[:, i, 1:2], EPS, None, ALU.add).then_inc(S["dve_ve2"], 1)
                dve.wait_ge(S["pool_r2"], i + 1)
                dve.tensor_scalar(yout[:, i, :], yout[:, i, :], mvar[:, i, 0:1], rstd[:, i:i + 1], ALU.subtract, ALU.mult
                                  ).then_inc(S["dve_y"], 1)

        @block.gpsimd
        def _(pool):
            pool.memset(mh[:, :], -0.5).then_inc(S["pool_c"], 1)
            pool.wait_ge(S["pool_c"], 1)
            pool.wait_ge(S["dve_ve"], 1)
            pool.tensor_tensor(rstd[:, :], rstd[:, :], mh[:, :], ALU.pow).then_inc(S["pool_r"], 1)

            def split(f, e):
                pool.wait_ge(S["act_gh"], f + 1)
                pool.tensor_tensor(gh[:, 1, e, :], gw[:, e, :], gh[:, 0, e, :], ALU.subtract).then_inc(S["pool_gl"], 1)
                pool.wait_ge(S["act_dh"], f + 1)
                o = bass.ds(f, 1)
                pool.tensor_tensor(dh[:, 1, o, :], dw[:, e, :].unsqueeze(1), dh[:, 0, o, :], ALU.subtract
                                   ).then_inc(S["pool_dl"], 1)

            split(0, 0)

            def body(f, e):
                if not isinstance(f, int) or f + 1 < NF:
                    split(f + 1, 1 - e)
                for half in range(2):
                    pool.wait_ge(S["act_hh"], 2 * f + half + 1)
                    hs = slice(half * TB, (half + 1) * TB)
                    o = bass.ds(f, 1)
                    pool.tensor_tensor(hf[:, 1, o, hs], sg[:, half, :].unsqueeze(1), hf[:, 0, o, hs], ALU.subtract
                                       ).then_inc(S["pool_hl"], 1)

            blocks(pool, body)
            for i in range(NT):
                pool.wait_ge(S["dve_ve2"], i + 1)
                pool.tensor_tensor(rstd[:, i:i + 1], rstd[:, i:i + 1], mh[:, 0:1], ALU.pow).then_inc(S["pool_r2"], 1)


def kernel(**inputs):
    import numpy as np
    import concourse.bacc as bacc
    from concourse.bass_utils import run_bass_kernel_spmd

    a = {k[3:]: np.asarray(v) for k, v in inputs.items()}
    w = a["attn_in_proj_w"]
    start = {"g": 0, "h": H * HP, "B": 2 * H * HP, "C": 2 * H * HP + G * P}
    width = {"g": GC, "h": GC, "B": P, "C": P}
    conv_w, conv_b = a["attn_conv_w"], a["attn_conv_b"]

    def rows(kind, m, g):
        o = start[kind] + g * width[kind] + m * P
        return slice(o, o + P)

    def by_k(block):
        return block.reshape(P, KD, P).transpose(2, 1, 0).reshape(P, KD * P)

    w_in = np.stack([by_k(w[rows(kind, m, g)]) for g in range(G) for kind, m in ORDER])
    convp = np.zeros((G, P, NC, 5), np.float32)
    for g in range(G):
        for i, (kind, m) in enumerate(CONV):
            r = rows(kind, m, g)
            r = slice(r.start - H * HP, r.stop - H * HP)
            convp[g, :, i, 0:4] = conv_w[r]
            convp[g, :, i, 4] = conv_b[r]
    d_rows = np.repeat(a["attn_Dp"], HP).reshape(G, NPAIR, P).transpose(0, 2, 1)
    gn_rows = a["attn_gnorm_w"].reshape(G, NPAIR, P).transpose(0, 2, 1)

    def gate_up(gate, up):
        both = np.stack([gate, up]).reshape(2, KD, P, NF, P)
        return both.transpose(3, 2, 0, 1, 4).reshape(NF, P, 2 * KD * P)

    def gate_up_rows(gate, up):
        return np.stack([gate, up]).reshape(2, KD, NF, P).transpose(2, 0, 1, 3).reshape(NF, 2 * KD * P)

    arrays = {
        "x": a["attn_x"].reshape(T, D),
        "w_in": w_in,
        "w_dt": by_k(w[PROJ_DT:PROJ_DT + H]),
        "convp": convp.reshape(G, P, NC * 5),
        "dpar": np.concatenate([d_rows, gn_rows], axis=2),
        "w_out": a["attn_out_proj_w"].T.reshape(G * NPAIR, P, D),
        "norm_w": a["attn_norm_w"].reshape(KD, P).T,
        "dt_bias": a["attn_dt_bias"].reshape(H, 1),
        "a_log": a["attn_A_log"].reshape(H, 1),
        "wgu": gate_up(a["ffn_gate_w"], a["ffn_up_w"]),
        "zgu": gate_up_rows(a["ffn_gate_z"], a["ffn_up_z"]),
        "sgu": gate_up_rows(a["ffn_gate_s"], a["ffn_up_s"]),
        "wdn": a["ffn_down_w"].reshape(NF, P, D),
        "zdn": a["ffn_down_z"],
        "sdn": a["ffn_down_s"],
    }
    arrays = {k: np.ascontiguousarray(v) for k, v in arrays.items()}
    nc = bacc.Bacc("TRN2", target_bir_lowering=False, num_devices=1, dynamic_dma_scratch_size=1024)
    aps = [nc.dram_tensor(k, v.shape, mybir.dt.from_np(v.dtype), kind="ExternalInput").ap() for k, v in arrays.items()]
    out = nc.dram_tensor("out", (T, D), F32, kind="ExternalOutput").ap()
    build(nc, *aps, out)
    r = run_bass_kernel_spmd(nc, [arrays], core_ids=[0])
    return r.results[0]["out"].reshape(2, TB, D)
```
